# Optimizing a Trainium2 kernel written in Bass

```python
import numpy as np
import jax
import jax.numpy as jnp

def _softmax(x, axis=-1):
    return jax.nn.softmax(x, axis=axis)

def _gelu(x):
    return jax.nn.gelu(x, approximate=True)

def _silu(x):
    return jax.nn.silu(x)

def _sigmoid(x):
    return jax.nn.sigmoid(x)

def _layernorm(x, axis=-1, eps=1e-05):
    m = jnp.mean(x, axis=axis, keepdims=True)
    v = jnp.var(x, axis=axis, keepdims=True)
    return (x - m) / jnp.sqrt(v + eps)

def _scatter_add(tgt, idx, src, axis=0):
    return tgt.at[idx].add(src)

def _segment_sum(src, seg, n):
    return jax.ops.segment_sum(src, seg, n)
kernel_name = 'mk_dlrm_tower_d1_rec_r8_07d3df'

def setup_inputs(seed: int=0):
    np.random.seed(seed)
    _w = jnp.asarray

    def _rec_inputs():
        import jax
        import jax.numpy as jnp
        _tk = jax.random.key(seed)
        dense_ctx = jax.random.normal(jax.random.fold_in(_tk, 190), (512, 16), jnp.float32)
        ids = jnp.stack([jax.random.randint(jax.random.fold_in(_tk, 200 + f), (512,), 0, v, jnp.int32) for f, v in enumerate([1250, 125000, 1000, 1000, 12500, 1250, 1250, 1250, 12500, 1250, 1250, 12500, 1000, 1250, 12500, 12500, 1000, 1000, 12500, 1000, 12500, 12500, 1250, 1250, 1000, 1000, 1250])], axis=1)
        tbl_0 = 0.05 * jax.random.normal(jax.random.fold_in(_tk, 500 + 0), (1250, 128), jnp.float32)
        tbl_1 = 0.05 * jax.random.normal(jax.random.fold_in(_tk, 500 + 1), (125000, 128), jnp.float32)
        tbl_2 = 0.05 * jax.random.normal(jax.random.fold_in(_tk, 500 + 2), (1000, 128), jnp.float32)
        tbl_3 = 0.05 * jax.random.normal(jax.random.fold_in(_tk, 500 + 3), (1000, 128), jnp.float32)
        tbl_4 = 0.05 * jax.random.normal(jax.random.fold_in(_tk, 500 + 4), (12500, 128), jnp.float32)
        tbl_5 = 0.05 * jax.random.normal(jax.random.fold_in(_tk, 500 + 5), (1250, 128), jnp.float32)
        tbl_6 = 0.05 * jax.random.normal(jax.random.fold_in(_tk, 500 + 6), (1250, 128), jnp.float32)
        tbl_7 = 0.05 * jax.random.normal(jax.random.fold_in(_tk, 500 + 7), (1250, 128), jnp.float32)
        tbl_8 = 0.05 * jax.random.normal(jax.random.fold_in(_tk, 500 + 8), (12500, 128), jnp.float32)
        tbl_9 = 0.05 * jax.random.normal(jax.random.fold_in(_tk, 500 + 9), (1250, 128), jnp.float32)
        tbl_10 = 0.05 * jax.random.normal(jax.random.fold_in(_tk, 500 + 10), (1250, 128), jnp.float32)
        tbl_11 = 0.05 * jax.random.normal(jax.random.fold_in(_tk, 500 + 11), (12500, 128), jnp.float32)
        tbl_12 = 0.05 * jax.random.normal(jax.random.fold_in(_tk, 500 + 12), (1000, 128), jnp.float32)
        tbl_13 = 0.05 * jax.random.normal(jax.random.fold_in(_tk, 500 + 13), (1250, 128), jnp.float32)
        tbl_14 = 0.05 * jax.random.normal(jax.random.fold_in(_tk, 500 + 14), (12500, 128), jnp.float32)
        tbl_15 = 0.05 * jax.random.normal(jax.random.fold_in(_tk, 500 + 15), (12500, 128), jnp.float32)
        tbl_16 = 0.05 * jax.random.normal(jax.random.fold_in(_tk, 500 + 16), (1000, 128), jnp.float32)
        tbl_17 = 0.05 * jax.random.normal(jax.random.fold_in(_tk, 500 + 17), (1000, 128), jnp.float32)
        tbl_18 = 0.05 * jax.random.normal(jax.random.fold_in(_tk, 500 + 18), (12500, 128), jnp.float32)
        tbl_19 = 0.05 * jax.random.normal(jax.random.fold_in(_tk, 500 + 19), (1000, 128), jnp.float32)
        tbl_20 = 0.05 * jax.random.normal(jax.random.fold_in(_tk, 500 + 20), (12500, 128), jnp.float32)
        tbl_21 = 0.05 * jax.random.normal(jax.random.fold_in(_tk, 500 + 21), (12500, 128), jnp.float32)
        tbl_22 = 0.05 * jax.random.normal(jax.random.fold_in(_tk, 500 + 22), (1250, 128), jnp.float32)
        tbl_23 = 0.05 * jax.random.normal(jax.random.fold_in(_tk, 500 + 23), (1250, 128), jnp.float32)
        tbl_24 = 0.05 * jax.random.normal(jax.random.fold_in(_tk, 500 + 24), (1000, 128), jnp.float32)
        tbl_25 = 0.05 * jax.random.normal(jax.random.fold_in(_tk, 500 + 25), (1000, 128), jnp.float32)
        tbl_26 = 0.05 * jax.random.normal(jax.random.fold_in(_tk, 500 + 26), (1250, 128), jnp.float32)
        _rk = jax.random.fold_in(_tk, 7)
        W_top1 = 0.0521996 * jax.random.normal(jax.random.fold_in(_tk, 801), (367, 512), jnp.float32)
        W_top2 = 0.0441942 * jax.random.normal(jax.random.fold_in(_tk, 802), (512, 256), jnp.float32)
        W_top3 = 0.0625 * jax.random.normal(jax.random.fold_in(_tk, 803), (256, 1), jnp.float32)
        b_top1 = jnp.zeros((512,), jnp.float32)
        b_top2 = jnp.zeros((256,), jnp.float32)
        return (dense_ctx, ids, tbl_0, tbl_1, tbl_2, tbl_3, tbl_4, tbl_5, tbl_6, tbl_7, tbl_8, tbl_9, tbl_10, tbl_11, tbl_12, tbl_13, tbl_14, tbl_15, tbl_16, tbl_17, tbl_18, tbl_19, tbl_20, tbl_21, tbl_22, tbl_23, tbl_24, tbl_25, tbl_26, W_top1, b_top1, W_top2, b_top2, W_top3)
    dense_ctx, ids, tbl_0, tbl_1, tbl_2, tbl_3, tbl_4, tbl_5, tbl_6, tbl_7, tbl_8, tbl_9, tbl_10, tbl_11, tbl_12, tbl_13, tbl_14, tbl_15, tbl_16, tbl_17, tbl_18, tbl_19, tbl_20, tbl_21, tbl_22, tbl_23, tbl_24, tbl_25, tbl_26, W_top1, b_top1, W_top2, b_top2, W_top3 = _rec_inputs()

    def _L0_rec_setup():
        import jax, jax.numpy as jnp
        import numpy as np

        def _tri_indices(num_feas):
            return np.array([i * num_feas + j for j in range(1, num_feas) for i in range(j)], dtype=np.int32)
        key = jax.random.key(seed)
        batch, num_feas, embed_dim = (2048, 27, 128)
        inputs = jax.random.normal(key, (batch, num_feas, embed_dim), dtype=jnp.float32)
        return {'inputs': inputs, 'num_feas': num_feas}
    _L0_rec_all = _L0_rec_setup()
    _L0_rec_in = {k: v for k, v in _L0_rec_all.items() if k in ()}
    del _L0_rec_all
    return {'dense_ctx': dense_ctx, 'ids': ids, 'tbl_0': tbl_0, 'tbl_1': tbl_1, 'tbl_2': tbl_2, 'tbl_3': tbl_3, 'tbl_4': tbl_4, 'tbl_5': tbl_5, 'tbl_6': tbl_6, 'tbl_7': tbl_7, 'tbl_8': tbl_8, 'tbl_9': tbl_9, 'tbl_10': tbl_10, 'tbl_11': tbl_11, 'tbl_12': tbl_12, 'tbl_13': tbl_13, 'tbl_14': tbl_14, 'tbl_15': tbl_15, 'tbl_16': tbl_16, 'tbl_17': tbl_17, 'tbl_18': tbl_18, 'tbl_19': tbl_19, 'tbl_20': tbl_20, 'tbl_21': tbl_21, 'tbl_22': tbl_22, 'tbl_23': tbl_23, 'tbl_24': tbl_24, 'tbl_25': tbl_25, 'tbl_26': tbl_26, 'W_top1': W_top1, 'b_top1': b_top1, 'W_top2': W_top2, 'b_top2': b_top2, 'W_top3': W_top3}

def reference(dense_ctx, ids, tbl_0, tbl_1, tbl_2, tbl_3, tbl_4, tbl_5, tbl_6, tbl_7, tbl_8, tbl_9, tbl_10, tbl_11, tbl_12, tbl_13, tbl_14, tbl_15, tbl_16, tbl_17, tbl_18, tbl_19, tbl_20, tbl_21, tbl_22, tbl_23, tbl_24, tbl_25, tbl_26, W_top1, b_top1, W_top2, b_top2, W_top3):
    import jax
    import jax.numpy as jnp

    def _L0_rec_ref(inputs, num_feas):
        import jax, jax.numpy as jnp
        import numpy as np

        def _tri_indices(num_feas):
            return np.array([i * num_feas + j for j in range(1, num_feas) for i in range(j)], dtype=np.int32)
        dot = jnp.einsum('bnd,bmd->bnm', inputs, inputs)
        idx = jnp.asarray(_tri_indices(num_feas))
        flat = dot.reshape(inputs.shape[0], num_feas * num_feas)
        return flat[:, idx]
    e = jnp.stack([tbl_0[ids[:, 0]], tbl_1[ids[:, 1]], tbl_2[ids[:, 2]], tbl_3[ids[:, 3]], tbl_4[ids[:, 4]], tbl_5[ids[:, 5]], tbl_6[ids[:, 6]], tbl_7[ids[:, 7]], tbl_8[ids[:, 8]], tbl_9[ids[:, 9]], tbl_10[ids[:, 10]], tbl_11[ids[:, 11]], tbl_12[ids[:, 12]], tbl_13[ids[:, 13]], tbl_14[ids[:, 14]], tbl_15[ids[:, 15]], tbl_16[ids[:, 16]], tbl_17[ids[:, 17]], tbl_18[ids[:, 18]], tbl_19[ids[:, 19]], tbl_20[ids[:, 20]], tbl_21[ids[:, 21]], tbl_22[ids[:, 22]], tbl_23[ids[:, 23]], tbl_24[ids[:, 24]], tbl_25[ids[:, 25]], tbl_26[ids[:, 26]]], axis=1)
    z = _L0_rec_ref(e, 27)
    z = z.reshape(z.shape[0], -1)
    h = jnp.concatenate([z, dense_ctx], axis=1)
    h = jnp.maximum(h @ W_top1 + b_top1, 0.0)
    h = jnp.maximum(h @ W_top2 + b_top2, 0.0)
    y = h @ W_top3
    return y

_drawn_inputs = setup_inputs


def setup_inputs(seed=0):
    import zlib

    import numpy as np

    out = dict(_drawn_inputs(seed))
    spreads = {'b_top1': (0.0, 0.1), 'b_top2': (0.0, 0.1)}
    factors = {}
    for name, (base, spread) in spreads.items():
        noise = np.random.default_rng([zlib.crc32(name.encode()), seed]).standard_normal(out[name].shape)
        drawn = base * np.exp(spread * noise) if base else spread * noise
        out[name] = jnp.asarray(drawn.astype(out[name].dtype))
    for name, factor in factors.items():
        out[name] = (out[name] * factor).astype(out[name].dtype)
    return out
```

```python
import concourse.bass as bass
import concourse.mybir as mybir
from contextlib import ExitStack

F32 = mybir.dt.float32
F32R = mybir.dt.float32r
I32 = mybir.dt.int32
ALU = mybir.AluOpType
ACT = mybir.ActivationFunctionType

P = 128
BATCH, D, DENSE = 512, 128, 16
H1, H2 = 512, 256
ROWS = [1250, 125000, 1000, 1000, 12500, 1250, 1250, 1250, 12500, 1250, 1250, 12500, 1000, 1250,
        12500, 12500, 1000, 1000, 12500, 1000, 12500, 12500, 1250, 1250, 1000, 1000, 1250]
NF = len(ROWS)
BLOCKS = BATCH // P

TP = 125
SMALL = [f for f in range(NF) if ROWS[f] == 1000] + [f for f in range(NF) if ROWS[f] == 1250][:1]
BIG = [f for f in range(NF) if f not in SMALL]
ORDER = SMALL + BIG
NS = len(SMALL)
CHUNKS = [ROWS[f] // TP for f in SMALL]
MAXCH = max(CHUNKS)
KINDS = sorted(set(CHUNKS))
DONE = [sum(CHUNKS[:t + 1]) for t in range(NS)]
RAWS, SPLITS, HOTS, EBANKS = 3, 2, 8, 3

GROUP = 4
GROUPS = [list(range(q, min(q + GROUP, NF))) for q in range(NS, NF, GROUP)]
EARLY = 2

ND = NF - 1
FOLDS = ND // 2
NPAIR = FOLDS * NF
ZW = NPAIR + DENSE
KCH = [(k, min(P, ZW - k)) for k in range(0, ZW, P)]
LANES = 32
QUADS = P // LANES
GCOLS = LANES // 2 * ND


def pair_rows():
    rows = []
    for k in range(FOLDS):
        for p in range(NF):
            a, b = (p, k + 1) if p <= k else (NF - 1 - p, NF - 1 - k)
            i, j = sorted((ORDER[a], ORDER[b]))
            rows.append(j * (j - 1) // 2 + i)
    return rows + list(range(NPAIR, ZW))


def build(nc, ids, small_ids, tables, dense, w1, b1, w2, b2, w3, out):
    ctx = ExitStack()
    with ctx:
        def sb(name, shape, dt=F32):
            return ctx.enter_context(nc.sbuf_tensor(name, shape, dt))

        def ps(name, shape):
            return ctx.enter_context(nc.psum_tensor(name, shape, F32))

        def sem(name):
            return ctx.enter_context(nc.semaphore(name))

        idx = sb("idx", [P, BLOCKS, NF], I32)
        sids = sb("sids", [TP, NS, BATCH], I32)
        raw = sb("raw", [TP, RAWS, MAXCH * D])
        hi = sb("hi", [TP, SPLITS, MAXCH * D], F32R)
        lo = sb("lo", [TP, SPLITS, MAXCH * D], F32R)
        hot = sb("hot", [TP, HOTS, BATCH], F32R)
        rowid = sb("rowid", [TP, len(KINDS), MAXCH])
        ident = sb("ident", [P, P])
        upper = sb("upper", [P, FOLDS, NF])
        got = sb("got", [P, BLOCKS, NF - NS, D])
        et_flat = sb("et_flat", [P, BATCH * NF + LANES - NF])
        et = et_flat[:, 0:BATCH * NF].rearrange("p (b q) -> p b q", q=NF)
        dots = sb("dots", [P, ND, LANES])
        z = sb("z", [P, BLOCKS, ZW])
        zt = sb("zt", [P, len(KCH), P])
        h1t = sb("h1t", [P, H1 // P, P])
        h2t = sb("h2t", [P, H2 // P, P])
        y = sb("y", [P, BLOCKS])
        w1s = sb("w1s", [P, len(KCH), H1])
        w2s = sb("w2s", [P, H1 // P, H2])
        w3s = sb("w3s", [P, H2 // P])
        b1s = sb("b1s", [P, H1 // P])
        b2s = sb("b2s", [P, H2 // P])

        emb = [ps(f"emb{i}", [P, BATCH]) for i in range(EBANKS)]
        gram = ps("gram", [P, 2, 512])
        hid = [ps(f"hid{i}", [P, 2, 256]) for i in range(2)]
        tail = ps("tail", [P, 512])

        idx_in = sem("idx_in")
        table_in = [sem(f"table_in{t}") for t in range(NS)]
        dense_in = sem("dense_in")
        w1_in, w2_in, vec_in = sem("w1_in"), sem("w2_in"), sem("vec_in")
        filled, consts, rows_made = sem("filled"), sem("consts"), sem("rows_made")
        pad_set = sem("pad_set")
        hi_made, lo_made = sem("hi_made"), sem("lo_made")
        hot_made, hot_used = sem("hot_made"), sem("hot_used")
        emb_full, emb_copied = sem("emb_full"), sem("emb_copied")
        gathered = [[sem(f"gathered{c}_{g}") for g in range(len(GROUPS))] for c in range(BLOCKS)]
        gram_full, dots_made = sem("gram_full"), sem("dots_made")
        folded, z_made = sem("folded"), sem("z_made")
        zt_full, zt_copied = sem("zt_full"), sem("zt_copied")
        h1_full, h1_made = sem("h1_full"), sem("h1_made")
        h2_full, h2_made = sem("h2_full"), sem("h2_made")
        y_full, y_copied, y_out = sem("y_full"), sem("y_copied"), sem("y_out")
        block = ctx.enter_context(nc.Block())

        @block.sync
        def _(sp):
            sp.dma_start(idx[:, :, :], ids.rearrange("(p c) f -> p c f", c=BLOCKS)).then_inc(idx_in, 16)
            for t in range(NS):
                if t >= RAWS:
                    sp.wait_ge(lo_made, t - RAWS + 1)
                sp.dma_start(raw[:, t % RAWS, 0:CHUNKS[t] * D],
                             tables[SMALL[t]].rearrange("(p c) d -> p (c d)", p=TP)).then_inc(table_in[t], 16)
                sp.dma_start(sids[:, t, :], small_ids[t, :].partition_broadcast(TP)).then_inc(table_in[t], 16)
                if t == RAWS - 1:
                    sp.dma_start(z[:, :, NPAIR:ZW], dense.rearrange("(p c) d -> p c d", c=BLOCKS)).then_inc(dense_in, 16)
                    for n, (k, rows) in enumerate(KCH):
                        sp.dma_start(w1s[0:rows, n, :], w1[k:k + rows, :]).then_inc(w1_in, 16)
                    sp.dma_start(w2s[:, :, :], w2.rearrange("(k p) m -> p k m", p=P)).then_inc(w2_in, 16)
                    sp.dma_start(w3s[:, :], w3).then_inc(vec_in, 16)
                    sp.dma_start(b1s[:, :], b1).then_inc(vec_in, 16)
                    sp.dma_start(b2s[:, :], b2).then_inc(vec_in, 16)
            sp.wait_ge(y_copied, BLOCKS)
            sp.dma_start(out.rearrange("(p c) o -> p (c o)", c=BLOCKS), y[:, :]).then_inc(y_out, 16)
            sp.wait_ge(y_out, 16)

        @block.gpsimd
        def _(pool):
            for n, ch in enumerate(KINDS):
                nc.gpsimd.iota(rowid[:, n, 0:ch], pattern=[[1, ch]], base=0, channel_multiplier=ch,
                               allow_small_or_imprecise_dtypes=True).then_inc(rows_made, 1)
            nc.gpsimd.memset(ident[:, :], 0.0).then_inc(filled, 1)
            nc.gpsimd.memset(upper[:, :, :], 0.0).then_inc(filled, 1)
            pool.wait_ge(filled, 2)
            nc.gpsimd.affine_select(out=ident[:, :], in_=ident[:, :], compare_op=ALU.not_equal, fill=1.0,
                                    base=0, pattern=[[-1, P]], channel_multiplier=1).then_inc(consts, 1)
            nc.gpsimd.affine_select(out=upper[:, :, :], in_=upper[:, :, :], compare_op=ALU.is_ge, fill=1.0,
                                    base=0, pattern=[[1, FOLDS], [-1, NF]], channel_multiplier=0).then_inc(consts, 1)
            pool.wait_ge(idx_in, 16)
            for c in range(BLOCKS):
                for g, slots in enumerate(GROUPS):
                    for q in slots:
                        pool.indirect_dma_start(got[:, c, q - NS, :], None, tables[ORDER[q]][:, :],
                                                bass.IndirectOffsetOnAxis(idx[:, c, ORDER[q]:ORDER[q] + 1], 0)
                                                ).then_inc(gathered[c][g], 16)

        @block.scalar
        def _(act):
            def split_high(t):
                act.wait_ge(table_in[t], 32)
                if t >= SPLITS:
                    act.wait_ge(hot_used, DONE[t - SPLITS])
                nc.scalar.activation(hi[:, t % SPLITS, 0:CHUNKS[t] * D], raw[:, t % RAWS, 0:CHUNKS[t] * D],
                                     ACT.Copy).then_inc(hi_made, 1)

            def copy_small(t):
                act.wait_ge(hot_used, DONE[t])
                nc.scalar.activation(et[:, :, t], emb[t % EBANKS][:, :], ACT.Copy).then_inc(emb_copied, 1)

            def copy_groups(c, which):
                for g in which:
                    n = NS + c * len(GROUPS) + g
                    slots = GROUPS[g]
                    act.wait_ge(emb_full, n - NS + 1)
                    nc.scalar.activation(
                        et[:, c * P:(c + 1) * P, slots[0]:slots[-1] + 1].rearrange("p b q -> p q b"),
                        emb[n % EBANKS][:, 0:len(slots) * P].rearrange("p (q b) -> p q b", b=P),
                        ACT.Copy).then_inc(emb_copied, 1)

            split_high(0)
            for t in range(NS):
                if t + 1 < NS:
                    split_high(t + 1)
                copy_small(t)
            all_groups = range(len(GROUPS))
            copy_groups(0, all_groups)
            act.wait_ge(vec_in, 48)
            for c in range(BLOCKS):
                if c + 1 < BLOCKS:
                    copy_groups(c + 1, all_groups[:EARLY])
                for half in range(2):
                    act.wait_ge(h1_full, 2 * c + half + 1)
                    for i in range(2):
                        m = 2 * half + i
                        last = nc.scalar.activation(h1t[:, m, :], hid[half][:, i, 0:P], ACT.Relu,
                                                    bias=b1s[:, m:m + 1])
                    last.then_inc(h1_made, 1)
                act.wait_ge(h2_full, c + 1)
                for m in range(H2 // P):
                    last = nc.scalar.activation(h2t[:, m, :], tail[:, m * P:(m + 1) * P], ACT.Relu,
                                                bias=b2s[:, m:m + 1])
                last.then_inc(h2_made, 1)
                if c + 1 < BLOCKS:
                    copy_groups(c + 1, all_groups[EARLY:])

        @block.vector
        def _(dve):
            nc.vector.memset(et_flat[:, BATCH * NF:], 0.0).then_inc(pad_set, 1)
            dve.wait_ge(rows_made, len(KINDS))
            n = 0
            for t in range(NS):
                dve.wait_ge(hi_made, t + 1)
                nc.vector.tensor_tensor(lo[:, t % SPLITS, 0:CHUNKS[t] * D], raw[:, t % RAWS, 0:CHUNKS[t] * D],
                                        hi[:, t % SPLITS, 0:CHUNKS[t] * D].bitcast(F32),
                                        ALU.subtract).then_inc(lo_made, 1)
                dve.wait_ge(table_in[t], 32)
                for ch in range(CHUNKS[t]):
                    if n >= HOTS:
                        dve.wait_ge(hot_used, n - HOTS + 1)
                    nc.vector.tensor_scalar(hot[:, n % HOTS, :], sids[:, t, :],
                                            rowid[:, KINDS.index(CHUNKS[t]), ch:ch + 1], None,
                                            ALU.is_equal).then_inc(hot_made, 1)
                    n += 1
            dve.wait_ge(consts, 2)
            for c in range(BLOCKS):
                dve.wait_ge(gram_full, c + 1)
                if c:
                    dve.wait_ge(z_made, c)
                nc.vector.transpose(dots[:, :, :].rearrange("p j (h g) -> p j h g", h=2),
                                    gram[:, :, 0:GCOLS].rearrange("p h (g j) -> p j h g", j=ND)
                                    ).then_inc(dots_made, 1)
                dve.wait_ge(dots_made, c + 1)
                line = z[:, c, 0:NPAIR].rearrange("p (k i) -> p k i", i=NF)
                nc.vector.tensor_copy(line, dots[:, 0:FOLDS, 0:NF]).then_inc(folded, 1)
                dve.wait_ge(folded, c + 1)
                nc.vector.copy_predicated(line, upper[:, :, :].bitcast(I32),
                                          dots[:, ND - 1:FOLDS - 1:-1, NF - 1::-1]).then_inc(z_made, 1)
                dve.wait_ge(zt_full, c + 1)
                for n, (k, rows) in enumerate(KCH):
                    last = nc.vector.tensor_copy(zt[0:rows, n, :], tail[0:rows, n * P:(n + 1) * P])
                last.then_inc(zt_copied, 1)
                dve.wait_ge(y_full, c + 1)
                nc.vector.tensor_copy(y[:, c:c + 1], tail[:, H2:H2 + 1]).then_inc(y_copied, 1)

        @block.tensor
        def _(pe):
            n = 0
            for t in range(NS):
                pe.wait_ge(lo_made, t + 1)
                if t >= EBANKS:
                    pe.wait_ge(emb_copied, t - EBANKS + 1)
                for ch in range(CHUNKS[t]):
                    pe.wait_ge(hot_made, n + 1)
                    for part in (hi, lo):
                        last = nc.tensor.matmul(emb[t % EBANKS][:, :],
                                                part[:, t % SPLITS, ch * D:(ch + 1) * D],
                                                hot[:, n % HOTS, :],
                                                start=(ch == 0 and part is hi),
                                                stop=(ch == CHUNKS[t] - 1 and part is lo))
                    last.then_inc(hot_used, 1)
                    n += 1

            def transpose_groups(c, which):
                for g in which:
                    n = NS + c * len(GROUPS) + g
                    pe.wait_ge(gathered[c][g], 16 * len(GROUPS[g]))
                    if n >= EBANKS:
                        pe.wait_ge(emb_copied, n - EBANKS + 1)
                    for i, q in enumerate(GROUPS[g]):
                        last = nc.tensor.transpose(emb[n % EBANKS][:, i * P:(i + 1) * P],
                                                   got[:, c, q - NS, :], ident[:, :])
                    last.then_inc(emb_full, 1)

            def all_dots(c):
                pe.wait_ge(emb_copied, NS + (c + 1) * len(GROUPS))
                if c:
                    pe.wait_ge(dots_made, c)
                for g in range(LANES):
                    for s in range(QUADS):
                        b = c * P + s * LANES + g
                        last = nc.tensor.matmul(
                            gram[s * LANES:(s + 1) * LANES, g // 16, g % 16 * ND:(g % 16 + 1) * ND],
                            et_flat[:, b * NF:b * NF + LANES], et[:, b, 1:NF], start=True, stop=True)
                last.then_inc(gram_full, 1)

            def layers(c):
                pe.wait_ge(z_made, c + 1)
                if c:
                    pe.wait_ge(y_copied, c)
                for n, (k, rows) in enumerate(KCH):
                    last = nc.tensor.transpose(tail[0:rows, n * P:(n + 1) * P], z[:, c, k:k + rows],
                                               ident[:, :])
                last.then_inc(zt_full, 1)
                pe.wait_ge(zt_copied, c + 1)
                for half in range(2):
                    if c:
                        pe.wait_ge(h1_made, 2 * (c - 1) + half + 1)
                    for i in range(2):
                        m = 2 * half + i
                        for n, (k, rows) in enumerate(KCH):
                            last = nc.tensor.matmul(hid[half][:, i, 0:P], w1s[0:rows, n, m * P:(m + 1) * P],
                                                    zt[0:rows, n, :], start=(n == 0), stop=(n == len(KCH) - 1))
                    last.then_inc(h1_full, 1)
                for m in range(H2 // P):
                    for k in range(H1 // P):
                        if m == 0 and k % 2 == 0:
                            pe.wait_ge(h1_made, 2 * c + k // 2 + 1)
                        last = nc.tensor.matmul(tail[:, m * P:(m + 1) * P], w2s[:, k, m * P:(m + 1) * P],
                                                h1t[:, k, :], start=(k == 0), stop=(k == H1 // P - 1))
                last.then_inc(h2_full, 1)
                pe.wait_ge(h2_made, c + 1)
                for k in range(H2 // P):
                    last = nc.tensor.matmul(tail[:, H2:H2 + 1], h2t[:, k, :], w3s[:, k:k + 1],
                                            start=(k == 0), stop=(k == H2 // P - 1))
                last.then_inc(y_full, 1)

            all_groups = range(len(GROUPS))
            pe.wait_ge(consts, 2)
            pe.wait_ge(pad_set, 1)
            pe.wait_ge(dense_in, 16)
            pe.wait_ge(w1_in, 16 * len(KCH))
            pe.wait_ge(w2_in, 16)
            pe.wait_ge(vec_in, 48)
            transpose_groups(0, all_groups)
            for c in range(BLOCKS):
                all_dots(c)
                if c + 1 < BLOCKS:
                    transpose_groups(c + 1, all_groups[:EARLY])
                layers(c)
                if c + 1 < BLOCKS:
                    transpose_groups(c + 1, all_groups[EARLY:])


def kernel(**inputs):
    import numpy as np
    import concourse.bacc as bacc
    from concourse.bass_utils import run_bass_kernel_spmd

    given = {name: np.asarray(a) for name, a in inputs.items()}
    ids = given["ids"]
    arrays = {
        "ids": ids,
        "small_ids": ids.reshape(P, BLOCKS, NF).transpose(2, 1, 0).reshape(NF, BATCH)[SMALL],
        "dense": given["dense_ctx"],
        "w1": given["W_top1"][pair_rows()],
        "b1": given["b_top1"].reshape(H1 // P, P).T,
        "w2": given["W_top2"],
        "b2": given["b_top2"].reshape(H2 // P, P).T,
        "w3": given["W_top3"].reshape(H2 // P, P).T,
    }
    for f in range(NF):
        arrays[f"tbl_{f}"] = given[f"tbl_{f}"]
    arrays = {f"in_{k}": np.ascontiguousarray(a) for k, a in arrays.items()}
    nc = bacc.Bacc("TRN2", target_bir_lowering=False, num_devices=1)
    aps = {name[3:]: nc.dram_tensor(name, a.shape, mybir.dt.from_np(a.dtype), kind="ExternalInput").ap()
           for name, a in arrays.items()}
    out = nc.dram_tensor("out_y", (BATCH, 1), F32, kind="ExternalOutput").ap()
    tables = [aps.pop(f"tbl_{f}") for f in range(NF)]
    build(nc, tables=tables, out=out, **aps)
    return run_bass_kernel_spmd(nc, [arrays], core_ids=[0]).results[0]["out_y"]
```

```python
import concourse.bass as bass
import concourse.mybir as mybir
from contextlib import ExitStack

F32 = mybir.dt.float32
F32R = mybir.dt.float32r
I32 = mybir.dt.int32
ALU = mybir.AluOpType
ACT = mybir.ActivationFunctionType

P = 128
BATCH, D, DENSE = 512, 128, 16
H1, H2 = 512, 256
ROWS = [1250, 125000, 1000, 1000, 12500, 1250, 1250, 1250, 12500, 1250, 1250, 12500, 1000, 1250,
        12500, 12500, 1000, 1000, 12500, 1000, 12500, 12500, 1250, 1250, 1000, 1000, 1250]
NF = len(ROWS)
BLOCKS = BATCH // P

TP = 125
SMALL = [f for f in range(NF) if ROWS[f] == 1000] + [f for f in range(NF) if ROWS[f] == 1250][:1]
BIG = [f for f in range(NF) if f not in SMALL]
ORDER = SMALL + BIG
NS = len(SMALL)
CHUNKS = [ROWS[f] // TP for f in SMALL]
MAXCH = max(CHUNKS)
KINDS = sorted(set(CHUNKS))
DONE = [sum(CHUNKS[:t + 1]) for t in range(NS)]
BYACT = 2
LOWAT = 1
RAWS, SPLITS, HOTS, EBANKS = 3, 2, 10, 3

GROUP = 4
GROUPS = [list(range(q, min(q + GROUP, NF))) for q in range(NS, NF, GROUP)]
CUTS = [(3, 4, 5), (3, 4, 5), (2, 3, 3)]

ND = NF - 1
FOLDS = ND // 2
NPAIR = FOLDS * NF
ZW = NPAIR + DENSE
KCH = [(k, min(P, ZW - k)) for k in range(0, ZW, P)]
LANES = 32
QUADS = P // LANES
GCOLS = LANES // 2 * ND


def pair_rows():
    rows = []
    for k in range(FOLDS):
        for p in range(NF):
            a, b = (p, k + 1) if p <= k else (NF - 1 - p, NF - 1 - k)
            i, j = sorted((ORDER[a], ORDER[b]))
            rows.append(j * (j - 1) // 2 + i)
    return rows + list(range(NPAIR, ZW))


def build(nc, ids, small_ids, tables, dense, w1, b1, w2, b2, w3, out):
    ctx = ExitStack()
    with ctx:
        def sb(name, shape, dt=F32):
            return ctx.enter_context(nc.sbuf_tensor(name, shape, dt))

        def ps(name, shape):
            return ctx.enter_context(nc.psum_tensor(name, shape, F32))

        def sem(name):
            return ctx.enter_context(nc.semaphore(name))

        idx = sb("idx", [P, BLOCKS, NF], I32)
        sids = sb("sids", [TP, RAWS, BATCH], I32)
        raw = sb("raw", [TP, RAWS, MAXCH * D])
        hi = sb("hi", [TP, SPLITS, MAXCH * D], F32R)
        lo = sb("lo", [TP, SPLITS, MAXCH * D], F32R)
        hot = sb("hot", [TP, HOTS, BATCH], F32R)
        square = sb("square", [TP, 2, BATCH])
        negrow = sb("negrow", [TP, len(KINDS), MAXCH])
        rowid = sb("rowid", [TP, len(KINDS), MAXCH])
        ident = sb("ident", [P, P])
        upper = sb("upper", [P, FOLDS, NF])
        got = sb("got", [P, BLOCKS, NF - NS, D])
        et_flat = sb("et_flat", [P, BATCH * NF + LANES - NF])
        et = et_flat[:, 0:BATCH * NF].rearrange("p (b q) -> p b q", q=NF)
        dots = sb("dots", [P, ND, LANES])
        z = sb("z", [P, BLOCKS, ZW])
        zt = sb("zt", [P, len(KCH), P])
        h1t = sb("h1t", [P, H1 // P, P])
        h2t = sb("h2t", [P, H2 // P, P])
        y = sb("y", [P, BLOCKS])
        w1s = sb("w1s", [P, len(KCH), H1])
        w2s = sb("w2s", [P, H1 // P, H2])
        w3s = sb("w3s", [P, H2 // P])
        b1s = sb("b1s", [P, H1 // P])
        b2s = sb("b2s", [P, H2 // P])

        emb = [ps(f"emb{i}", [P, BATCH]) for i in range(EBANKS)]
        gram = ps("gram", [P, 2, 512])
        hid = [ps(f"hid{i}", [P, 2, 256]) for i in range(2)]
        tail = ps("tail", [P, 512])

        idx_in = sem("idx_in")
        table_in = [sem(f"table_in{t}") for t in range(NS)]
        sids_in = [sem(f"sids_in{t}") for t in range(NS)]
        dense_in = sem("dense_in")
        w1_in, w2_in, vec_in = sem("w1_in"), sem("w2_in"), sem("vec_in")
        filled, consts, rows_made = sem("filled"), sem("consts"), sem("rows_made")
        pad_set = sem("pad_set")
        hi_made, lo_made = sem("hi_made"), sem("lo_made")
        hot_made, act_hot_made, hot_used = sem("hot_made"), sem("act_hot_made"), sem("hot_used")
        squared = sem("squared")
        emb_full, emb_copied = sem("emb_full"), sem("emb_copied")
        gathered = [[sem(f"gathered{c}_{g}") for g in range(len(GROUPS))] for c in range(BLOCKS)]
        gram_full, dots_made = sem("gram_full"), sem("dots_made")
        folded, z_made = sem("folded"), sem("z_made")
        zt_full, zt_copied = sem("zt_full"), sem("zt_copied")
        h1_full, h1_made = sem("h1_full"), sem("h1_made")
        h2_full, h2_made = sem("h2_full"), sem("h2_made")
        y_full, y_copied, y_out = sem("y_full"), sem("y_copied"), sem("y_out")
        block = ctx.enter_context(nc.Block())

        @block.sync
        def _(sp):
            sp.dma_start(idx[:, :, :], ids.rearrange("(p c) f -> p c f", c=BLOCKS)).then_inc(idx_in, 16)
            for t in range(NS):
                if t >= RAWS:
                    sp.wait_ge(hot_used, DONE[t - RAWS])
                sp.dma_start(sids[:, t % RAWS, :], small_ids[t, :].partition_broadcast(TP)).then_inc(sids_in[t], 16)
                sp.dma_start(raw[:, t % RAWS, 0:CHUNKS[t] * D],
                             tables[SMALL[t]].rearrange("(p c) d -> p (c d)", p=TP)).then_inc(table_in[t], 16)
                if t == RAWS - 1:
                    sp.dma_start(z[:, :, NPAIR:ZW], dense.rearrange("(p c) d -> p c d", c=BLOCKS)).then_inc(dense_in, 16)
                    for n, (k, rows) in enumerate(KCH):
                        sp.dma_start(w1s[0:rows, n, :], w1[k:k + rows, :]).then_inc(w1_in, 16)
                    sp.dma_start(w2s[:, :, :], w2.rearrange("(k p) m -> p k m", p=P)).then_inc(w2_in, 16)
                    sp.dma_start(w3s[:, :], w3).then_inc(vec_in, 16)
                    sp.dma_start(b1s[:, :], b1).then_inc(vec_in, 16)
                    sp.dma_start(b2s[:, :], b2).then_inc(vec_in, 16)
            sp.wait_ge(y_copied, BLOCKS)
            sp.dma_start(out.rearrange("(p c) o -> p (c o)", c=BLOCKS), y[:, :]).then_inc(y_out, 16)
            sp.wait_ge(y_out, 16)

        @block.gpsimd
        def _(pool):
            for n, ch in enumerate(KINDS):
                nc.gpsimd.iota(rowid[:, n, 0:ch], pattern=[[1, ch]], base=0, channel_multiplier=ch,
                               allow_small_or_imprecise_dtypes=True).then_inc(rows_made, 1)
                nc.gpsimd.iota(negrow[:, n, 0:ch], pattern=[[-1, ch]], base=0, channel_multiplier=-ch,
                               allow_small_or_imprecise_dtypes=True).then_inc(rows_made, 1)
            nc.gpsimd.memset(ident[:, :], 0.0).then_inc(filled, 1)
            nc.gpsimd.memset(upper[:, :, :], 0.0).then_inc(filled, 1)
            pool.wait_ge(filled, 2)
            nc.gpsimd.affine_select(out=ident[:, :], in_=ident[:, :], compare_op=ALU.not_equal, fill=1.0,
                                    base=0, pattern=[[-1, P]], channel_multiplier=1).then_inc(consts, 1)
            nc.gpsimd.affine_select(out=upper[:, :, :], in_=upper[:, :, :], compare_op=ALU.is_ge, fill=1.0,
                                    base=0, pattern=[[1, FOLDS], [-1, NF]], channel_multiplier=0).then_inc(consts, 1)
            pool.wait_ge(idx_in, 16)
            for c in range(BLOCKS):
                for g, slots in enumerate(GROUPS):
                    for q in slots:
                        pool.indirect_dma_start(got[:, c, q - NS, :], None, tables[ORDER[q]][:, :],
                                                bass.IndirectOffsetOnAxis(idx[:, c, ORDER[q]:ORDER[q] + 1], 0)
                                                ).then_inc(gathered[c][g], 16)

        @block.scalar
        def _(act):
            def split_high(t):
                act.wait_ge(table_in[t], 16)
                if t >= SPLITS:
                    act.wait_ge(hot_used, DONE[t - SPLITS])
                nc.scalar.activation(hi[:, t % SPLITS, 0:CHUNKS[t] * D], raw[:, t % RAWS, 0:CHUNKS[t] * D],
                                     ACT.Copy).then_inc(hi_made, 1)

            def copy_small(t):
                act.wait_ge(hot_used, DONE[t])
                nc.scalar.activation(et[:, :, t], emb[t % EBANKS][:, :], ACT.Copy).then_inc(emb_copied, 1)

            def copy_groups(c, which):
                for g in which:
                    n = NS + c * len(GROUPS) + g
                    slots = GROUPS[g]
                    act.wait_ge(emb_full, n - NS + 1)
                    nc.scalar.activation(
                        et[:, c * P:(c + 1) * P, slots[0]:slots[-1] + 1].rearrange("p b q -> p q b"),
                        emb[n % EBANKS][:, 0:len(slots) * P].rearrange("p (q b) -> p q b", b=P),
                        ACT.Copy).then_inc(emb_copied, 1)

            def one_hots(t):
                act.wait_ge(sids_in[t], 16)
                for i in range(BYACT):
                    ch, m = CHUNKS[t] - BYACT + i, BYACT * t + i
                    if m >= 2:
                        act.wait_ge(act_hot_made, m - 1)
                    nc.scalar.activation(square[:, m % 2, :], sids[:, t % RAWS, :], ACT.Square,
                                         bias=negrow[:, KINDS.index(CHUNKS[t]), ch:ch + 1]
                                         ).then_inc(squared, 1)
                for i in range(BYACT):
                    n, m = DONE[t] - BYACT + i, BYACT * t + i
                    act.wait_ge(squared, m + 1)
                    if n >= HOTS:
                        act.wait_ge(hot_used, n - HOTS + 1)
                    nc.scalar.activation(hot[:, n % HOTS, :], square[:, m % 2, :], ACT.Relu,
                                         bias=1.0, scale=-1.0).then_inc(act_hot_made, 1)

            act.wait_ge(rows_made, 2 * len(KINDS))
            split_high(0)
            one_hots(0)
            for t in range(NS):
                if t + 1 < NS:
                    split_high(t + 1)
                    one_hots(t + 1)
                copy_small(t)
            all_groups = range(len(GROUPS))
            copy_groups(0, all_groups)
            act.wait_ge(vec_in, 48)
            for c in range(BLOCKS):
                before_z, before_1, before_2 = CUTS[c] if c + 1 < BLOCKS else (0, 0, 0)
                if c + 1 < BLOCKS:
                    copy_groups(c + 1, all_groups[:before_1])
                for half in range(2):
                    act.wait_ge(h1_full, 2 * c + half + 1)
                    for i in range(2):
                        m = 2 * half + i
                        last = nc.scalar.activation(h1t[:, m, :], hid[half][:, i, 0:P], ACT.Relu,
                                                    bias=b1s[:, m:m + 1])
                    last.then_inc(h1_made, 1)
                if c + 1 < BLOCKS:
                    copy_groups(c + 1, all_groups[before_1:before_2])
                act.wait_ge(h2_full, c + 1)
                for m in range(H2 // P):
                    last = nc.scalar.activation(h2t[:, m, :], tail[:, m * P:(m + 1) * P], ACT.Relu,
                                                bias=b2s[:, m:m + 1])
                last.then_inc(h2_made, 1)
                if c + 1 < BLOCKS:
                    copy_groups(c + 1, all_groups[before_2:])

        @block.vector
        def _(dve):
            nc.vector.memset(et_flat[:, BATCH * NF:], 0.0).then_inc(pad_set, 1)
            dve.wait_ge(rows_made, 2 * len(KINDS))
            for t in range(NS):
                dve.wait_ge(sids_in[t], 16)
                for ch in range(CHUNKS[t] - BYACT):
                    if ch == LOWAT:
                        dve.wait_ge(hi_made, t + 1)
                        nc.vector.tensor_tensor(
                            lo[:, t % SPLITS, 0:CHUNKS[t] * D], raw[:, t % RAWS, 0:CHUNKS[t] * D],
                            hi[:, t % SPLITS, 0:CHUNKS[t] * D].bitcast(F32), ALU.subtract).then_inc(lo_made, 1)
                    n = DONE[t] - CHUNKS[t] + ch
                    if n >= HOTS:
                        dve.wait_ge(hot_used, n - HOTS + 1)
                    nc.vector.tensor_scalar(hot[:, n % HOTS, :], sids[:, t % RAWS, :],
                                            rowid[:, KINDS.index(CHUNKS[t]), ch:ch + 1], None,
                                            ALU.is_equal).then_inc(hot_made, 1)
            dve.wait_ge(consts, 2)
            for c in range(BLOCKS):
                dve.wait_ge(gram_full, c + 1)
                if c:
                    dve.wait_ge(z_made, c)
                nc.vector.transpose(dots[:, :, :].rearrange("p j (h g) -> p j h g", h=2),
                                    gram[:, :, 0:GCOLS].rearrange("p h (g j) -> p j h g", j=ND)
                                    ).then_inc(dots_made, 1)
                dve.wait_ge(dots_made, c + 1)
                line = z[:, c, 0:NPAIR].rearrange("p (k i) -> p k i", i=NF)
                nc.vector.tensor_copy(line, dots[:, 0:FOLDS, 0:NF]).then_inc(folded, 1)
                dve.wait_ge(folded, c + 1)
                nc.vector.copy_predicated(line, upper[:, :, :].bitcast(I32),
                                          dots[:, ND - 1:FOLDS - 1:-1, NF - 1::-1]).then_inc(z_made, 1)
                dve.wait_ge(zt_full, c + 1)
                for n, (k, rows) in enumerate(KCH):
                    last = nc.vector.tensor_copy(zt[0:rows, n, :], tail[0:rows, n * P:(n + 1) * P])
                last.then_inc(zt_copied, 1)
                dve.wait_ge(y_full, c + 1)
                nc.vector.tensor_copy(y[:, c:c + 1], tail[:, H2:H2 + 1]).then_inc(y_copied, 1)

        @block.tensor
        def _(pe):
            n = 0
            for t in range(NS):
                pe.wait_ge(lo_made, t + 1)
                if t >= EBANKS:
                    pe.wait_ge(emb_copied, t - EBANKS + 1)
                for ch in range(CHUNKS[t]):
                    act_ch = ch - (CHUNKS[t] - BYACT)
                    if act_ch < 0:
                        pe.wait_ge(hot_made, n - BYACT * t + 1)
                    else:
                        pe.wait_ge(act_hot_made, BYACT * t + act_ch + 1)
                    for part in (hi, lo):
                        last = nc.tensor.matmul(emb[t % EBANKS][:, :],
                                                part[:, t % SPLITS, ch * D:(ch + 1) * D],
                                                hot[:, n % HOTS, :],
                                                start=(ch == 0 and part is hi),
                                                stop=(ch == CHUNKS[t] - 1 and part is lo))
                    last.then_inc(hot_used, 1)
                    n += 1

            def transpose_groups(c, which):
                for g in which:
                    n = NS + c * len(GROUPS) + g
                    pe.wait_ge(gathered[c][g], 16 * len(GROUPS[g]))
                    if n >= EBANKS:
                        pe.wait_ge(emb_copied, n - EBANKS + 1)
                    for i, q in enumerate(GROUPS[g]):
                        last = nc.tensor.transpose(emb[n % EBANKS][:, i * P:(i + 1) * P],
                                                   got[:, c, q - NS, :], ident[:, :])
                    last.then_inc(emb_full, 1)

            def all_dots(c):
                pe.wait_ge(emb_copied, NS + (c + 1) * len(GROUPS))
                if c:
                    pe.wait_ge(dots_made, c)
                for g in range(LANES):
                    for s in range(QUADS):
                        b = c * P + s * LANES + g
                        last = nc.tensor.matmul(
                            gram[s * LANES:(s + 1) * LANES, g // 16, g % 16 * ND:(g % 16 + 1) * ND],
                            et_flat[:, b * NF:b * NF + LANES], et[:, b, 1:NF], start=True, stop=True)
                last.then_inc(gram_full, 1)

            def transpose_z(c):
                pe.wait_ge(z_made, c + 1)
                if c:
                    pe.wait_ge(y_copied, c)
                for n, (k, rows) in enumerate(KCH):
                    last = nc.tensor.transpose(tail[0:rows, n * P:(n + 1) * P], z[:, c, k:k + rows],
                                               ident[:, :])
                last.then_inc(zt_full, 1)

            def layer_1(c):
                pe.wait_ge(zt_copied, c + 1)
                for half in range(2):
                    if c:
                        pe.wait_ge(h1_made, 2 * (c - 1) + half + 1)
                    for i in range(2):
                        m = 2 * half + i
                        for n, (k, rows) in enumerate(KCH):
                            last = nc.tensor.matmul(hid[half][:, i, 0:P], w1s[0:rows, n, m * P:(m + 1) * P],
                                                    zt[0:rows, n, :], start=(n == 0), stop=(n == len(KCH) - 1))
                    last.then_inc(h1_full, 1)

            def layer_2(c):
                for m in range(H2 // P):
                    for k in range(H1 // P):
                        if m == 0 and k % 2 == 0:
                            pe.wait_ge(h1_made, 2 * c + k // 2 + 1)
                        last = nc.tensor.matmul(tail[:, m * P:(m + 1) * P], w2s[:, k, m * P:(m + 1) * P],
                                                h1t[:, k, :], start=(k == 0), stop=(k == H1 // P - 1))
                last.then_inc(h2_full, 1)

            def layer_3(c):
                pe.wait_ge(h2_made, c + 1)
                for k in range(H2 // P):
                    last = nc.tensor.matmul(tail[:, H2:H2 + 1], h2t[:, k, :], w3s[:, k:k + 1],
                                            start=(k == 0), stop=(k == H2 // P - 1))
                last.then_inc(y_full, 1)

            all_groups = range(len(GROUPS))
            pe.wait_ge(consts, 2)
            pe.wait_ge(pad_set, 1)
            pe.wait_ge(dense_in, 16)
            pe.wait_ge(w1_in, 16 * len(KCH))
            pe.wait_ge(w2_in, 16)
            pe.wait_ge(vec_in, 48)
            transpose_groups(0, all_groups)
            for c in range(BLOCKS):
                before_z, before_1, before_2 = CUTS[c] if c + 1 < BLOCKS else (0, 0, 0)
                all_dots(c)
                if c + 1 < BLOCKS:
                    transpose_groups(c + 1, all_groups[:before_z])
                transpose_z(c)
                if c + 1 < BLOCKS:
                    transpose_groups(c + 1, all_groups[before_z:before_1])
                layer_1(c)
                if c + 1 < BLOCKS:
                    transpose_groups(c + 1, all_groups[before_1:before_2])
                layer_2(c)
                if c + 1 < BLOCKS:
                    transpose_groups(c + 1, all_groups[before_2:])
                layer_3(c)


def kernel(**inputs):
    import numpy as np
    import concourse.bacc as bacc
    from concourse.bass_utils import run_bass_kernel_spmd

    given = {name: np.asarray(a) for name, a in inputs.items()}
    ids = given["ids"]
    arrays = {
        "ids": ids,
        "small_ids": ids.reshape(P, BLOCKS, NF).transpose(2, 1, 0).reshape(NF, BATCH)[SMALL],
        "dense": given["dense_ctx"],
        "w1": given["W_top1"][pair_rows()],
        "b1": given["b_top1"].reshape(H1 // P, P).T,
        "w2": given["W_top2"],
        "b2": given["b_top2"].reshape(H2 // P, P).T,
        "w3": given["W_top3"].reshape(H2 // P, P).T,
    }
    for f in range(NF):
        arrays[f"tbl_{f}"] = given[f"tbl_{f}"]
    arrays = {f"in_{k}": np.ascontiguousarray(a) for k, a in arrays.items()}
    nc = bacc.Bacc("TRN2", target_bir_lowering=False, num_devices=1)
    aps = {name[3:]: nc.dram_tensor(name, a.shape, mybir.dt.from_np(a.dtype), kind="ExternalInput").ap()
           for name, a in arrays.items()}
    out = nc.dram_tensor("out_y", (BATCH, 1), F32, kind="ExternalOutput").ap()
    tables = [aps.pop(f"tbl_{f}") for f in range(NF)]
    build(nc, tables=tables, out=out, **aps)
    return run_bass_kernel_spmd(nc, [arrays], core_ids=[0]).results[0]["out_y"]
```
